# Optimizing a Trainium2 kernel written in Bass

```python
import numpy as np
import jax
import jax.numpy as jnp

def _softmax(x, axis=-1):
    return jax.nn.softmax(x, axis=axis)

def _gelu(x):
    return jax.nn.gelu(x, approximate=True)

def _silu(x):
    return jax.nn.silu(x)

def _sigmoid(x):
    return jax.nn.sigmoid(x)

def _layernorm(x, axis=-1, eps=1e-05):
    m = jnp.mean(x, axis=axis, keepdims=True)
    v = jnp.var(x, axis=axis, keepdims=True)
    return (x - m) / jnp.sqrt(v + eps)

def _scatter_add(tgt, idx, src, axis=0):
    return tgt.at[idx].add(src)

def _segment_sum(src, seg, n):
    return jax.ops.segment_sum(src, seg, n)
kernel_name = 'mk_rec_standalone_d1_rec_r8_fbc810'

def setup_inputs(seed: int=0):
    np.random.seed(seed)
    _w = jnp.asarray

    def _rec_inputs():
        import jax
        import jax.numpy as jnp
        _rk = jax.random.key(seed)
        r_target_key = -0.00154741 + 1.00114 * jax.random.normal(jax.random.fold_in(_rk, 1), (512, 64), jnp.float32)
        r_item_keys = -0.00010897 + 0.999902 * jax.random.normal(jax.random.fold_in(_rk, 2), (512, 200, 64), jnp.float32)
        r_item_values = 0.000157846 + 1.00013 * jax.random.normal(jax.random.fold_in(_rk, 3), (512, 200, 64), jnp.float32)
        r_mask = jax.random.randint(jax.random.fold_in(_rk, 4), (512, 200), 0, 2, jnp.int32)
        return (r_target_key, r_item_keys, r_item_values, r_mask)
    r_target_key, r_item_keys, r_item_values, r_mask = _rec_inputs()

    def _L0_rec_setup():
        import jax, jax.numpy as jnp
        import numpy as np
        B, L, D = (512, 200, 64)
        key = jax.random.key(seed)
        ks = jax.random.split(key, 7)
        target_key = jax.random.normal(ks[0], (B, D), dtype=jnp.float32)
        item_keys = jax.random.normal(ks[1], (B, L, D), dtype=jnp.float32)
        item_values = jax.random.normal(ks[2], (B, L, D), dtype=jnp.float32)
        mask = jax.random.randint(ks[3], (B, L), 0, 2, dtype=jnp.int32)
        scale = 1.0 / np.sqrt(D)
        W_target = jax.random.uniform(ks[4], (D, D), jnp.float32, -scale, scale)
        W_item = jax.random.uniform(ks[5], (D, D), jnp.float32, -scale, scale)
        W_value = jax.random.uniform(ks[6], (D, D), jnp.float32, -scale, scale)
        return {'target_key': target_key, 'item_keys': item_keys, 'item_values': item_values, 'mask': mask, 'W_target': W_target, 'W_item': W_item, 'W_value': W_value}
    _L0_rec_all = _L0_rec_setup()
    _L0_rec_in = {k: v for k, v in _L0_rec_all.items() if k in ('W_target', 'W_item', 'W_value')}
    del _L0_rec_all
    return {'r_target_key': r_target_key, 'r_item_keys': r_item_keys, 'r_item_values': r_item_values, 'r_mask': r_mask, 'L0_rec_W_target': _L0_rec_in['W_target'], 'L0_rec_W_item': _L0_rec_in['W_item'], 'L0_rec_W_value': _L0_rec_in['W_value']}

def reference(r_target_key, r_item_keys, r_item_values, r_mask, L0_rec_W_target, L0_rec_W_item, L0_rec_W_value):
    import jax
    import jax.numpy as jnp

    def _L0_rec_ref(target_key, item_keys, item_values, mask, W_target, W_item, W_value):
        import jax, jax.numpy as jnp
        import numpy as np
        B, L, D = (512, 200, 64)
        scaler = jnp.float32(D) ** 0.5
        q = target_key @ W_target.T
        k = jnp.einsum('bld,ed->ble', item_keys, W_item)
        v = jnp.einsum('bld,ed->ble', item_values, W_value)
        scores = jnp.einsum('bd,bld->bl', q, k) / scaler
        scores = scores + -100000000.0 * (1.0 - mask.astype(scores.dtype))
        w = jax.nn.softmax(scores, axis=1)
        return jnp.einsum('bl,bld->bd', w, v)
    y = _L0_rec_ref(r_target_key, r_item_keys, r_item_values, r_mask, L0_rec_W_target, L0_rec_W_item, L0_rec_W_value)
    return y

_drawn_inputs = setup_inputs


def setup_inputs(seed=0):
    import zlib

    import numpy as np

    out = dict(_drawn_inputs(seed))
    spreads = {}
    factors = {}
    for name, (base, spread) in spreads.items():
        noise = np.random.default_rng([zlib.crc32(name.encode()), seed]).standard_normal(out[name].shape)
        drawn = base * np.exp(spread * noise) if base else spread * noise
        out[name] = jnp.asarray(drawn.astype(out[name].dtype))
    for name, factor in factors.items():
        out[name] = (out[name] * factor).astype(out[name].dtype)
    return out
```

```python
from contextlib import ExitStack

import concourse.bass as bass
from concourse import mybir

ALU = mybir.AluOpType
ACT = mybir.ActivationFunctionType
F32 = mybir.dt.float32
AX_X = mybir.AxisListType.X

P = 128
CH = 8
TB = P // CH
BT = 8
GT = 4
GB = BT // GT
KILL = -1.0e38
MASKED = 1.0e8


def masked_attention_kernel(nc, target, keys, values, mask, w_target, w_item, w_value, out):
    B, L, D = keys.shape
    JL = L // CH
    NP = (JL + 1) // 2
    NS = 2 * NP
    NT = B // TB
    NBLK = NT // BT
    NPA = (NP + 1) // 2
    NPB = NP - NPA
    UB = BT * TB
    assert 2 * D == P and JL * CH == L and JL % 2 == 1 and NT % BT == 0 and UB == P and B <= 512

    pair_item = [min(2 * k, JL - 2) for k in range(NP)]

    keys_tiled = keys.rearrange("(t b) (c j) d -> t (b c) (j d)", b=TB, c=CH)
    values_tiled = values.rearrange("(t b) (c j) d -> t (b c) (j d)", b=TB, c=CH)
    mask_tiled = mask.rearrange("(t b) (c j) -> (b c) t j", b=TB, c=CH)
    out_blocks = out.rearrange("(n u) d -> n u d", u=UB)

    with ExitStack() as ctx:
        def sb(name, shape, dt=F32):
            return ctx.enter_context(nc.sbuf_tensor(name, shape, dt))

        def psum(name, shape):
            return ctx.enter_context(nc.psum_tensor(name, shape, F32))

        def sem(name):
            return ctx.enter_context(nc.semaphore(name))

        key_ring = sb("key_ring", [P, BT, JL * D])
        value_ring = sb("value_ring", [P, BT, JL * D])
        ident = sb("ident", [P, P])
        own_user = sb("own_user", [P, TB])
        ones = sb("ones", [P, 1])
        target_sb = sb("target_sb", [P, B // P, D])
        w_target_sb = sb("w_target_sb", [D, D])
        w_item_twice = sb("w_item_twice", [D, 2, D])
        w_value_twice = sb("w_value_twice", [D, 2, D])
        target_t = sb("target_t", [D, B])
        w_target_t = sb("w_target_t", [D, D])
        w_value_t = sb("w_value_t", [P, D])
        query_t = sb("query_t", [D, B])
        query_diag = sb("query_diag", [P, NT, 2, TB])
        mask_sb = sb("mask_sb", [P, NT, JL], mask.dtype)
        mask_bias = sb("mask_bias", [P, NT, NS])
        keys_t_a = sb("keys_t_a", [P, NPA * P])
        keys_t_b = sb("keys_t_b", [P, NPB * P])
        picked = sb("picked", [P, NS, TB])
        scores = sb("scores", [P, BT, NS])
        chunk_max = sb("chunk_max", [P, BT])
        user_max = sb("user_max", [GT, TB])
        user_max_rep = sb("user_max_rep", [GT, TB, CH])
        expd = sb("expd", [P, BT, NS])
        exp_sum = sb("exp_sum", [P, BT])
        weights_diag = sb("weights_diag", [P, BT, NS, TB])
        exp_sum_diag = sb("exp_sum_diag", [P, BT, TB])
        context_t = sb("context_t", [P, BT, TB])
        inv_sum = sb("inv_sum", [P, 1])
        result = sb("result", [P, D])

        ps_keys_a = psum("ps_keys_a", [P, 1024])
        ps_keys_b = psum("ps_keys_b", [P, 1024])
        ps_scores = psum("ps_scores", [P, 2, 512])
        ps_context = psum("ps_context", [P, 512])
        ps_misc = psum("ps_misc", [P, 512])
        ps_max_t = ps_misc[0:GT, 0:P]
        ps_max_back = ps_misc[:, P:P + GT]
        ps_sum = ps_misc[:, P + GT:P + GT + 1]
        ps_project = ps_misc[:, 192:192 + D]
        ps_w_target_t = ps_misc[0:D, 256:256 + D]
        ps_w_value_t = ps_misc[:, 320:320 + D]
        ps_target_t = ps_scores[0:D, 0, 0:B]
        ps_query_t = ps_scores[0:D, 1, 0:B]
        ps_query2 = ps_context[:, 0:B]
        context_cols = ps_context[:, 0:BT * 2 * TB].rearrange("p (s j b) -> p s j b", s=BT, j=2)

        s_targets = sem("s_targets")
        s_weights = sem("s_weights")
        s_mask = sem("s_mask")
        s_key = [sem(f"s_key{s}") for s in range(BT)]
        s_value = [sem(f"s_value{s}") for s in range(BT)]
        s_fill = sem("s_fill")
        s_ident = sem("s_ident")
        s_own = sem("s_own")
        s_zeroed = sem("s_zeroed")
        s_small_t = sem("s_small_t")
        s_small_t_copied = sem("s_small_t_copied")
        s_query = sem("s_query")
        s_query_copied = sem("s_query_copied")
        s_query2 = sem("s_query2")
        s_query_diag = sem("s_query_diag")
        s_mask_bias = sem("s_mask_bias")
        s_keys_a = sem("s_keys_a")
        s_keys_b = sem("s_keys_b")
        s_copied_a = sem("s_copied_a")
        s_copied_b = sem("s_copied_b")
        s_scored_a = sem("s_scored_a")
        s_scored_b = sem("s_scored_b")
        s_picked = sem("s_picked")
        s_scores = sem("s_scores")
        s_biased = sem("s_biased")
        s_chunk_max = sem("s_chunk_max")
        s_max_t = sem("s_max_t")
        s_user_max = sem("s_user_max")
        s_user_max_rep = sem("s_user_max_rep")
        s_max_back = sem("s_max_back")
        s_shifted = sem("s_shifted")
        s_exp = sem("s_exp")
        s_exp_sum = sem("s_exp_sum")
        s_spread = sem("s_spread")
        s_weighted = sem("s_weighted")
        s_sum_diag = sem("s_sum_diag")
        s_sum = sem("s_sum")
        s_inv_sum = sem("s_inv_sum")
        s_context = sem("s_context")
        s_project = sem("s_project")
        s_result = sem("s_result")
        s_stored = sem("s_stored")

        block = ctx.enter_context(nc.Block())

        @block.sync
        def _(sp):
            def load_key(i, s, first):
                if not first:
                    sp.wait_ge(s_keys_b, BT * (i - 1) + s + 1)
                sp.dma_start(key_ring[:, s, :], keys_tiled[i * BT + s]).then_inc(s_key[s], 16)

            def load_value(i, s, first):
                if not first:
                    sp.wait_ge(s_weighted, BT * (i - 1) + s + 1)
                sp.dma_start(value_ring[:, s, :], values_tiled[i * BT + s]).then_inc(s_value[s], 16)

            for s in range(BT):
                load_key(0, s, True)
            for s in range(BT):
                load_key(1, s, False)
                load_value(0, s, True)
            with sp.Fori(2, NBLK) as i:
                for s in range(BT):
                    load_key(i, s, False)
                    load_value(i - 1, s, False)
            for s in range(BT):
                load_value(NBLK - 1, s, False)

        @block.gpsimd
        def _(pool):
            nc.gpsimd.memset(ident[:], 0.0).then_inc(s_fill, 1)
            pool.wait_ge(s_fill, 1)
            nc.gpsimd.affine_select(out=ident[:], in_=ident[:], compare_op=ALU.not_equal, fill=1.0, base=0,
                                    pattern=[[-1, P]], channel_multiplier=1).then_inc(s_ident, 1)
            nc.gpsimd.memset(own_user[:], 1.0).then_inc(s_fill, 1)
            pool.wait_ge(s_fill, 2)
            nc.gpsimd.affine_select(out=own_user[:], in_=own_user[:], compare_op=ALU.is_ge, fill=0.0, base=0,
                                    pattern=[[-CH, TB]], channel_multiplier=1).then_inc(s_fill, 1)
            pool.wait_ge(s_fill, 3)
            nc.gpsimd.affine_select(out=own_user[:], in_=own_user[:], compare_op=ALU.is_ge, fill=0.0, base=CH - 1,
                                    pattern=[[CH, TB]], channel_multiplier=-1).then_inc(s_own, 1)
            pool.wait_ge(s_own, 1)

            def spread(i, s, first):
                if s % GT == 0:
                    pool.wait_ge(s_exp, GB * i + s // GT + 1)
                if not first:
                    pool.wait_ge(s_weighted, BT * (i - 1) + s + 1)
                nc.gpsimd.tensor_tensor(
                    weights_diag[:, s], expd[:, s, :].unsqueeze(2).to_broadcast([P, NS, TB]),
                    own_user[:].unsqueeze(1).to_broadcast([P, NS, TB]), ALU.mult).then_inc(s_spread, 1)

            for s in range(BT):
                spread(0, s, True)
            with pool.Fori(1, NBLK) as i:
                for s in range(BT):
                    spread(i, s, False)

        @block.scalar
        def _(act):
            act.dma_start(target_sb[:], target.rearrange("(n p) d -> p n d", p=P)).then_inc(s_targets, 16)
            act.dma_start(w_target_sb[:], w_target).then_inc(s_weights, 16)
            for j in range(2):
                act.dma_start(w_item_twice[:, j], w_item).then_inc(s_weights, 16)
                act.dma_start(w_value_twice[:, j], w_value).then_inc(s_weights, 16)
            act.dma_start(mask_sb[:], mask_tiled).then_inc(s_mask, 16)

            act.wait_ge(s_small_t, 1)
            nc.scalar.copy(target_t[:], ps_target_t).then_inc(s_small_t_copied, 1)
            act.wait_ge(s_query, 1)
            nc.scalar.mul(query_t[:], ps_query_t, float(D) ** -0.5).then_inc(s_query_copied, 1)

            def step(i, s, first):
                t = BT * i + s
                act.wait_ge(s_keys_a, t + 1)
                if not (first and s == 0):
                    act.wait_ge(s_scored_a, t)
                nc.scalar.copy(keys_t_a[:], ps_keys_a[:, 0:NPA * P]).then_inc(s_copied_a, 1)
                if s == 2 and not first:
                    exp_group(GB * i - 1, GB - 1)
                if s == 2 + GT:
                    exp_group(GB * i, 0)
                act.wait_ge(s_keys_b, t + 1)
                if not (first and s == 0):
                    act.wait_ge(s_scored_b, t)
                nc.scalar.copy(keys_t_b[:], ps_keys_b[:, 0:NPB * P]).then_inc(s_copied_b, 1)

            def exp_group(g, half):
                act.wait_ge(s_shifted, g + 1)
                rows = slice(half * GT, half * GT + GT)
                nc.scalar.activation(expd[:, rows, :], scores[:, rows, :], ACT.Exp).then_inc(s_exp, 1)

            def store(i):
                act.wait_ge(s_result, i + 1)
                act.dma_start(out_blocks[i], result[:]).then_inc(s_stored, 16)

            for s in range(BT):
                step(0, s, True)
            with act.Fori(1, NBLK) as i:
                for s in range(BT):
                    step(i, s, False)
                store(i - 1)
            exp_group(GB * NBLK - 1, GB - 1)
            store(NBLK - 1)
            act.wait_ge(s_stored, 16 * NBLK)

        @block.vector
        def _(dve):
            nc.vector.memset(ones[:], 1.0).then_inc(s_zeroed, 1)
            nc.vector.memset(query_diag[:], 0.0).then_inc(s_zeroed, 1)
            nc.vector.memset(mask_bias[:], KILL).then_inc(s_zeroed, 1)
            dve.wait_ge(s_small_t, 2)
            nc.vector.tensor_copy(w_target_t[:], ps_w_target_t).then_inc(s_small_t_copied, 1)
            nc.vector.tensor_copy(w_value_t[:], ps_w_value_t).then_inc(s_small_t_copied, 1)
            dve.wait_ge(s_query2, 1)
            dve.wait_ge(s_zeroed, 3)
            for j in range(2):
                half = slice(j * D, j * D + D)
                nc.vector.tensor_copy(query_diag[half, :, j, :],
                                      ps_query2[half, :].rearrange("p (t b) -> p t b", b=TB)).then_inc(s_query_diag, 1)
            dve.wait_ge(s_mask, 16)
            nc.vector.tensor_scalar(mask_bias[:, :, 0:JL - 1], mask_sb[:, :, 0:JL - 1], -1.0, MASKED,
                                    ALU.add, ALU.mult).then_inc(s_mask_bias, 1)
            nc.vector.tensor_scalar(mask_bias[:, :, NS - 1:NS], mask_sb[:, :, JL - 1:JL], -1.0, MASKED,
                                    ALU.add, ALU.mult).then_inc(s_mask_bias, 1)
            dve.wait_ge(s_own, 1)
            dve.wait_ge(s_mask_bias, 2)

            def pick_scores(i, s, first):
                t = BT * i + s
                dve.wait_ge(s_scored_b, t + 1)
                if not (first and s == 0):
                    dve.wait_ge(s_scores, t)
                products = ps_scores[:, s % 2, 0:NS * TB].rearrange("p (n b) -> p n b", b=TB)
                nc.vector.tensor_tensor(picked[:], products, own_user[:].unsqueeze(1).to_broadcast([P, NS, TB]),
                                        ALU.mult).then_inc(s_picked, 1)
                dve.wait_ge(s_picked, t + 1)
                nc.vector.tensor_reduce(scores[:, s, :], picked[:], AX_X, ALU.add).then_inc(s_scores, 1)

            def bias_and_chunk_max(i, h):
                g = GB * i + h
                rows = slice(h * GT, h * GT + GT)
                dve.wait_ge(s_scores, GT * (g + 1))
                nc.vector.tensor_tensor(scores[:, rows, :], scores[:, rows, :],
                                        mask_bias[:, bass.ds(g * GT, GT), :], ALU.add).then_inc(s_biased, 1)
                dve.wait_ge(s_biased, g + 1)
                nc.vector.tensor_reduce(chunk_max[:, rows], scores[:, rows, :], AX_X, ALU.max).then_inc(s_chunk_max, 1)

            def user_maxima(g):
                dve.wait_ge(s_max_t, g + 1)
                nc.vector.tensor_reduce(user_max[:], ps_max_t.rearrange("t (b c) -> t b c", c=CH), AX_X,
                                        ALU.max).then_inc(s_user_max, 1)
                dve.wait_ge(s_user_max, g + 1)
                nc.vector.tensor_copy(user_max_rep[:], user_max[:].unsqueeze(2).to_broadcast([GT, TB, CH])) \
                    .then_inc(s_user_max_rep, 1)

            def shift(g, h):
                rows = slice(h * GT, h * GT + GT)
                dve.wait_ge(s_max_back, g + 1)
                nc.vector.tensor_tensor(scores[:, rows, :], scores[:, rows, :],
                                        ps_max_back.unsqueeze(2).to_broadcast([P, GT, NS]),
                                        ALU.subtract).then_inc(s_shifted, 1)

            def sum_exponentials(g, h, after_sum):
                rows = slice(h * GT, h * GT + GT)
                dve.wait_ge(s_exp, g + 1)
                nc.vector.tensor_reduce(exp_sum[:, rows], expd[:, rows, :], AX_X, ALU.add).then_inc(s_exp_sum, 1)
                dve.wait_ge(s_exp_sum, g + 1)
                if after_sum is not None:
                    dve.wait_ge(s_sum, after_sum)
                nc.vector.tensor_tensor(exp_sum_diag[:, rows, :], exp_sum[:, rows].unsqueeze(2).to_broadcast([P, GT, TB]),
                                        own_user[:].unsqueeze(1).to_broadcast([P, GT, TB]),
                                        ALU.mult).then_inc(s_sum_diag, 1)

            def invert_sums(i, first):
                dve.wait_ge(s_sum, i + 1)
                if not first:
                    dve.wait_ge(s_result, i)
                nc.vector.reciprocal(inv_sum[:], ps_sum).then_inc(s_inv_sum, 1)

            def copy_context(i):
                dve.wait_ge(s_weighted, BT * (i + 1))
                for j in range(2):
                    half = slice(j * D, j * D + D)
                    nc.vector.tensor_copy(context_t[half, :, :], context_cols[half, :, j, :]).then_inc(s_context, 1)
            def finish(i, first):
                dve.wait_ge(s_inv_sum, i + 1)
                dve.wait_ge(s_project, i + 1)
                if not first:
                    dve.wait_ge(s_stored, 16 * i)
                nc.vector.tensor_scalar(result[:], ps_project, inv_sum[:, 0:1], None, ALU.mult).then_inc(s_result, 1)

            def step(i, s, first, peeled):
                if s == 0 and not first:
                    user_maxima(GB * i - 1)
                if s == GT:
                    user_maxima(GB * i)
                if s == BT - 1 and not first:
                    invert_sums(i - 1, peeled)
                    copy_context(i - 1)
                pick_scores(i, s, first)
                if s == 1 and not first:
                    shift(GB * i - 1, GB - 1)
                if s == 1 + GT:
                    shift(GB * i, 0)
                if s == 3 and not first:
                    sum_exponentials(GB * i - 1, GB - 1, None)
                if s == 3 + GT:
                    sum_exponentials(GB * i, 0, None if first else i)
                if s % GT == GT - 1:
                    bias_and_chunk_max(i, s // GT)

            for s in range(BT):
                step(0, s, True, True)
            for s in range(BT):
                step(1, s, False, True)
            finish(0, True)
            with dve.Fori(2, NBLK) as i:
                for s in range(BT):
                    step(i, s, False, False)
                finish(i - 1, False)
            user_maxima(GB * NBLK - 1)
            shift(GB * NBLK - 1, GB - 1)
            sum_exponentials(GB * NBLK - 1, GB - 1, None)
            invert_sums(NBLK - 1, False)
            copy_context(NBLK - 1)
            finish(NBLK - 1, False)

        @block.tensor
        def _(pe):
            pe.wait_ge(s_ident, 1)
            pe.wait_ge(s_targets, 16)
            for n in range(B // P):
                last = nc.tensor.transpose(ps_target_t[:, n * P:(n + 1) * P], target_sb[:, n, :], ident[:])
            last.then_inc(s_small_t, 1)
            pe.wait_ge(s_weights, 16 * 5)
            nc.tensor.transpose(ps_w_target_t, w_target_sb[:], ident[0:D, 0:D])
            nc.tensor.transpose(ps_w_value_t, w_value_twice[:].rearrange("e j d -> e (j d)"),
                                ident[0:D, 0:D]).then_inc(s_small_t, 1)
            pe.wait_ge(s_small_t_copied, 3)
            nc.tensor.matmul(ps_query_t, w_target_t[:], target_t[:], start=True, stop=True).then_inc(s_query, 1)
            pe.wait_ge(s_query_copied, 1)
            nc.tensor.matmul(ps_query2, w_item_twice[:].rearrange("e j d -> e (j d)"), query_t[:],
                             start=True, stop=True).then_inc(s_query2, 1)

            def transpose_keys(i, s, first, part):
                t = BT * i + s
                if part == 0:
                    pe.wait_ge(s_key[s], 16 * (i + 1))
                pairs, dst, copied, done = ((range(NPA), ps_keys_a, s_copied_a, s_keys_a),
                                            (range(NPA, NP), ps_keys_b, s_copied_b, s_keys_b))[part]
                if not (first and s == 0):
                    pe.wait_ge(copied, t)
                for n, k in enumerate(pairs):
                    c = pair_item[k] * D
                    last = nc.tensor.transpose(dst[:, n * P:(n + 1) * P], key_ring[:, s, c:c + P], ident[:])
                last.then_inc(done, 1)

            def score(i, s, first, part):
                t = BT * i + s
                pairs, src, copied, done = ((range(NPA), keys_t_a, s_copied_a, s_scored_a),
                                            (range(NPA, NP), keys_t_b, s_copied_b, s_scored_b))[part]
                pe.wait_ge(copied, t + 1)
                if part == 0:
                    if first and s == 0:
                        pe.wait_ge(s_query_diag, 2)
                    if not (first and s < 2):
                        pe.wait_ge(s_picked, t - 1)
                query = query_diag[:, t].rearrange("p j b -> p (j b)") if isinstance(t, int) else \
                    query_diag[:, bass.ds(t, 1)].rearrange("p t j b -> p (t j b)")
                for n, k in enumerate(pairs):
                    last = nc.tensor.matmul(ps_scores[:, s % 2, k * 2 * TB:(k + 1) * 2 * TB],
                                            src[:, n * P:(n + 1) * P], query, start=True, stop=True)
                last.then_inc(done, 1)

            def weigh_values(i, s, first, part):
                if part == 0:
                    pe.wait_ge(s_value[s], 16 * (i + 1))
                    pe.wait_ge(s_spread, BT * i + s + 1)
                    if s == 0 and not first:
                        pe.wait_ge(s_context, 2 * i)
                for k in (range(NPA), range(NPA, NP))[part]:
                    c = pair_item[k] * D
                    last = nc.tensor.matmul(
                        ps_context[:, s * 2 * TB:(s + 1) * 2 * TB], value_ring[:, s, c:c + P],
                        weights_diag[:, s, 2 * k:2 * k + 2, :].rearrange("p n b -> p (n b)"),
                        start=(k == 0), stop=(k == NP - 1))
                if part == 1:
                    last.then_inc(s_weighted, 1)

            def turn_maxima(g, h, results):
                pe.wait_ge(s_chunk_max, g + 1)
                if results is not None:
                    pe.wait_ge(s_result, results)
                nc.tensor.matmul(ps_max_t, chunk_max[:, h * GT:(h + 1) * GT], ident[:],
                                 start=True, stop=True).then_inc(s_max_t, 1)

            def turn_back(g):
                pe.wait_ge(s_user_max_rep, g + 1)
                nc.tensor.matmul(ps_max_back, user_max_rep[:].rearrange("t b c -> t (b c)"), ident[0:GT, 0:GT],
                                 start=True, stop=True).then_inc(s_max_back, 1)

            def sum_by_user(i, shifted):
                pe.wait_ge(s_sum_diag, GB * (i + 1))
                pe.wait_ge(s_shifted, shifted)
                nc.tensor.matmul(ps_sum, exp_sum_diag[:].rearrange("p s b -> p (s b)"), ones[:],
                                 start=True, stop=True).then_inc(s_sum, 1)

            def project(i):
                pe.wait_ge(s_context, 2 * (i + 1))
                pe.wait_ge(s_inv_sum, i + 1)
                nc.tensor.matmul(ps_project, context_t[:].rearrange("p s b -> p (s b)"), w_value_t[:],
                                 start=True, stop=True).then_inc(s_project, 1)

            def step(i, s, first, peeled):
                transpose_keys(i, s, first, 0)
                if s > 0:
                    score(i, s - 1, first, 1)
                if s == 1 and not first:
                    turn_back(GB * i - 1)
                if s == 1 + GT:
                    turn_back(GB * i)
                if not first:
                    weigh_values(i - 1, s, peeled, 0)
                transpose_keys(i, s, first, 1)
                score(i, s, first, 0)
                if not first:
                    weigh_values(i - 1, s, peeled, 1)
                if s == 6 and not first:
                    sum_by_user(i - 1, GB * i + 1)
                if s == BT - 1:
                    score(i, s, first, 1)
                if s == 0 and not first:
                    turn_maxima(GB * i - 1, GB - 1, None if peeled else i - 1)
                if s == GT:
                    turn_maxima(GB * i, 0, None)

            for s in range(BT):
                step(0, s, True, True)
            for s in range(BT):
                step(1, s, False, True)
            project(0)
            with pe.Fori(2, NBLK) as i:
                for s in range(BT):
                    step(i, s, False, False)
                project(i - 1)
            for s in range(BT):
                weigh_values(NBLK - 1, s, False, 0)
                weigh_values(NBLK - 1, s, False, 1)
                if s == 0:
                    turn_maxima(GB * NBLK - 1, GB - 1, NBLK - 1)
                if s == 1:
                    turn_back(GB * NBLK - 1)
            sum_by_user(NBLK - 1, GB * NBLK)
            project(NBLK - 1)


_INS = ["r_target_key", "r_item_keys", "r_item_values", "r_mask", "L0_rec_W_target", "L0_rec_W_item", "L0_rec_W_value"]


def kernel(**inputs):
    import numpy as np
    import concourse.bacc as bacc
    from concourse.bass_utils import run_bass_kernel_spmd

    nc = bacc.Bacc("TRN2", target_bir_lowering=False, num_devices=1)
    arrays, args = {}, []
    for name in _INS:
        a = np.ascontiguousarray(inputs[name])
        arrays[f"{name}_dram"] = a
        args.append(nc.dram_tensor(f"{name}_dram", a.shape, mybir.dt.from_np(a.dtype), kind="ExternalInput").ap())
    shape = inputs["r_target_key"].shape
    out = nc.dram_tensor("out_dram", shape, F32, kind="ExternalOutput").ap()
    masked_attention_kernel(nc, *args, out)
    r = run_bass_kernel_spmd(nc, [arrays], core_ids=[0])
    return r.results[0]["out_dram"]
```

```python
from contextlib import ExitStack

import concourse.bass as bass
from concourse import mybir

ALU = mybir.AluOpType
ACT = mybir.ActivationFunctionType
F32 = mybir.dt.float32
AX_X = mybir.AxisListType.X

P = 128
CH = 8
TB = P // CH
BT = 8
GT = 4
GB = BT // GT
JW = 4
PT = 2
POOL_SLOTS = (2, 6)
MASKED = 1.0e8


def masked_attention_kernel(nc, target, keys, values, mask, w_target, w_item, w_value, out):
    B, L, D = keys.shape
    JL = L // CH
    NW = -(-JL // JW)
    NT = B // TB
    NBLK = NT // BT
    UB = BT * TB
    R = PT * TB
    NPAIR = BT // PT
    NPOOL = len(POOL_SLOTS)
    NVEC = BT - NPOOL
    assert JL * CH == L and NT % BT == 0 and UB == P and R * JW == P and NBLK >= 3
    assert JL - (NW - 1) * JW == 1 and BT * D == 512

    keys_tiled = keys.rearrange("(t b) (c j) d -> t (b c) (j d)", b=TB, c=CH)
    values_tiled = values.rearrange("(t b) (c j) d -> t (b c) (j d)", b=TB, c=CH)
    mask_tiled = mask.rearrange("(t b) (c j) -> (b c) t j", b=TB, c=CH)
    out_blocks = out.rearrange("(n u) d -> n u d", u=UB)

    def vector_products(i, s):
        return NVEC * i + len([x for x in range(s + 1) if x not in POOL_SLOTS])

    def pool_products(i, s):
        return NPOOL * i + len([x for x in range(s + 1) if x in POOL_SLOTS])

    with ExitStack() as ctx:
        def sb(name, shape, dt=F32):
            return ctx.enter_context(nc.sbuf_tensor(name, shape, dt))

        def psum(name, shape):
            return ctx.enter_context(nc.psum_tensor(name, shape, F32))

        def sem(name):
            return ctx.enter_context(nc.semaphore(name))

        key_ring = sb("key_ring", [P, BT, JL * D])
        value_ring = sb("value_ring", [P, BT, JL * D])
        ident = sb("ident", [P, P])
        own_user = sb("own_user", [P, TB])
        fold = sb("fold", [P, R])
        ones = sb("ones", [P, 1])
        target_sb = sb("target_sb", [P, B // P, D])
        w_target_sb = sb("w_target_sb", [D, D])
        w_item_sb = sb("w_item_sb", [D, D])
        w_value_sb = sb("w_value_sb", [D, D])
        target_t = sb("target_t", [D, B])
        w_target_t = sb("w_target_t", [D, D])
        w_value_t = sb("w_value_t", [D, D])
        query_t = sb("query_t", [D, NBLK, UB, CH])
        query_pool = sb("query_pool", [P, NBLK, NPOOL, D])
        mask_sb = sb("mask_sb", [P, NT, JL], mask.dtype)
        mask_bias = sb("mask_bias", [P, NT, JL])
        product = sb("product", [P, JL, D])
        product_pool = sb("product_pool", [P, NPOOL, JL, D])
        scores = sb("scores", [P, BT, JL])
        chunk_max = sb("chunk_max", [P, BT])
        user_max = sb("user_max", [GT, TB])
        user_max_rep = sb("user_max_rep", [GT, TB, CH])
        expd = sb("expd", [P, BT, JL])
        exp_sum = sb("exp_sum", [P, BT])
        weights = sb("weights", [P, BT, NW * JW, R])
        exp_sum_own = sb("exp_sum_own", [P, BT, TB])
        context = sb("context", [P, 2, D])
        context_t = sb("context_t", [D, UB])
        inv_sum = sb("inv_sum", [P, 1])
        result = sb("result", [P, D])

        ps_query = psum("ps_query", [P, NBLK, BT, D])
        ps_context = psum("ps_context", [P, 2, 512])
        ps_small = psum("ps_small", [P, 512])
        ps_out = psum("ps_out", [P, 512])
        ps_max_t = ps_small[0:GT, 0:P]
        ps_max_back = ps_small[:, P:P + GT]
        ps_sum = ps_small[:, P + GT:P + GT + 1]
        ps_w_target_t = ps_small[0:D, 256:256 + D]
        ps_w_value_t = ps_small[0:D, 256 + D:256 + 2 * D]
        ps_context_t = ps_out[0:D, 0:UB]
        ps_project = ps_out[:, UB:UB + D]
        ps_target_t = ps_context[0:D, 0, 0:B]
        ps_query_t = ps_context[0:D, 1, 0:B]

        s_targets = sem("s_targets")
        s_weights = sem("s_weights")
        s_mask = sem("s_mask")
        s_key = [sem(f"s_key{s}") for s in range(BT)]
        s_value = [sem(f"s_value{s}") for s in range(BT)]
        s_fill = sem("s_fill")
        s_ident = sem("s_ident")
        s_own = sem("s_own")
        s_ones = sem("s_ones")
        s_fold = sem("s_fold")
        s_small_t = sem("s_small_t")
        s_small_t_copied = sem("s_small_t_copied")
        s_query_t = sem("s_query_t")
        s_query_t_copied = sem("s_query_t_copied")
        s_query = sem("s_query")
        s_query_pool = sem("s_query_pool")
        s_mask_bias = sem("s_mask_bias")
        s_product = sem("s_product")
        s_product_pool = sem("s_product_pool")
        s_scores = sem("s_scores")
        s_biased = sem("s_biased")
        s_chunk_max = sem("s_chunk_max")
        s_max_t = sem("s_max_t")
        s_user_max = sem("s_user_max")
        s_user_max_rep = sem("s_user_max_rep")
        s_max_back = sem("s_max_back")
        s_shifted = sem("s_shifted")
        s_exp = sem("s_exp")
        s_spread = sem("s_spread")
        s_sum_own = sem("s_sum_own")
        s_weighted = sem("s_weighted")
        s_context = sem("s_context")
        s_context_t = sem("s_context_t")
        s_context_t_copied = sem("s_context_t_copied")
        s_sum = sem("s_sum")
        s_inv_sum = sem("s_inv_sum")
        s_project = sem("s_project")
        s_result = sem("s_result")
        s_stored = sem("s_stored")

        block = ctx.enter_context(nc.Block())

        @block.sync
        def _(sp):
            def load_key(i, s, first):
                if not first and s in POOL_SLOTS:
                    sp.wait_ge(s_product_pool, pool_products(i - 1, s))
                elif not first:
                    sp.wait_ge(s_product, vector_products(i - 1, s))
                sp.dma_start(key_ring[:, s, :], keys_tiled[i * BT + s]).then_inc(s_key[s], 16)

            def load_value(i, s, first):
                if not first:
                    sp.wait_ge(s_weighted, BT * (i - 1) + s + 1)
                sp.dma_start(value_ring[:, s, :], values_tiled[i * BT + s]).then_inc(s_value[s], 16)

            for s in range(BT):
                load_key(0, s, True)
            for s in range(BT):
                load_key(1, s, False)
                load_value(0, s, True)
            with sp.Fori(2, NBLK) as i:
                for s in range(BT):
                    load_key(i, s, False)
                    load_value(i - 1, s, False)
            for s in range(BT):
                load_value(NBLK - 1, s, False)

        @block.gpsimd
        def _(pool):
            nc.gpsimd.memset(ident[:], 0.0).then_inc(s_fill, 1)
            pool.wait_ge(s_fill, 1)
            nc.gpsimd.affine_select(out=ident[:], in_=ident[:], compare_op=ALU.not_equal, fill=1.0, base=0,
                                    pattern=[[-1, P]], channel_multiplier=1).then_inc(s_ident, 1)
            nc.gpsimd.memset(own_user[:], 1.0).then_inc(s_fill, 1)
            pool.wait_ge(s_fill, 2)
            nc.gpsimd.affine_select(out=own_user[:], in_=own_user[:], compare_op=ALU.is_ge, fill=0.0, base=0,
                                    pattern=[[-CH, TB]], channel_multiplier=1).then_inc(s_fill, 1)
            pool.wait_ge(s_fill, 3)
            nc.gpsimd.affine_select(out=own_user[:], in_=own_user[:], compare_op=ALU.is_ge, fill=0.0, base=CH - 1,
                                    pattern=[[CH, TB]], channel_multiplier=-1).then_inc(s_own, 1)
            nc.gpsimd.memset(weights[:], 0.0).then_inc(s_fill, 1)
            pool.wait_ge(s_own, 1)
            pool.wait_ge(s_fill, 4)

            def multiply(i, n, first):
                s = POOL_SLOTS[n]
                pool.wait_ge(s_key[s], 16 * (i + 1))
                if first:
                    pool.wait_ge(s_query_pool, NBLK)
                else:
                    pool.wait_ge(s_scores, BT * (i - 1) + s + 1)
                keys_s = key_ring[:, s, :].rearrange("p (j d) -> p j d", d=D)
                query = query_pool[:, bass.ds(i, 1), n, :].to_broadcast([P, JL, D])
                nc.gpsimd.tensor_tensor(product_pool[:, n], keys_s, query, ALU.mult).then_inc(s_product_pool, 1)

            def spread(i, h, first):
                g = GB * i + h
                pool.wait_ge(s_exp, GT * (g + 1))
                for s in range(h * GT, h * GT + GT):
                    if not first:
                        pool.wait_ge(s_weighted, BT * (i - 1) + s + 1)
                    users = slice(s % PT * TB, s % PT * TB + TB)
                    nc.gpsimd.tensor_tensor(
                        weights[:, s, 0:JL, users], expd[:, s, :].unsqueeze(2).to_broadcast([P, JL, TB]),
                        own_user[:].unsqueeze(1).to_broadcast([P, JL, TB]), ALU.mult).then_inc(s_spread, 1)
                rows = slice(h * GT, h * GT + GT)
                if not first:
                    pool.wait_ge(s_sum, i)
                nc.gpsimd.tensor_tensor(
                    exp_sum_own[:, rows, :], exp_sum[:, rows].unsqueeze(2).to_broadcast([P, GT, TB]),
                    own_user[:].unsqueeze(1).to_broadcast([P, GT, TB]), ALU.mult).then_inc(s_sum_own, 1)

            multiply(0, 0, True)
            multiply(0, 1, True)
            spread(0, 0, True)
            multiply(1, 0, False)
            spread(0, 1, True)
            multiply(1, 1, False)
            spread(1, 0, False)
            with pool.Fori(2, NBLK) as i:
                multiply(i, 0, False)
                spread(i - 1, 1, False)
                multiply(i, 1, False)
                spread(i, 0, False)
            spread(NBLK - 1, 1, False)

        @block.scalar
        def _(act):
            act.dma_start(target_sb[:], target.rearrange("(n p) d -> p n d", p=P)).then_inc(s_targets, 16)
            act.dma_start(w_target_sb[:], w_target).then_inc(s_weights, 16)
            act.dma_start(w_item_sb[:], w_item).then_inc(s_weights, 16)
            act.dma_start(w_value_sb[:], w_value).then_inc(s_weights, 16)
            act.dma_start(mask_sb[:], mask_tiled).then_inc(s_mask, 16)

            act.wait_ge(s_small_t, 1)
            nc.scalar.copy(target_t[:], ps_target_t).then_inc(s_small_t_copied, 1)
            act.wait_ge(s_query_t, 1)
            for i in range(NBLK):
                nc.scalar.mul(query_t[:, i], ps_query_t[:, i * UB:(i + 1) * UB].unsqueeze(2).to_broadcast([D, UB, CH]),
                              float(D) ** -0.5).then_inc(s_query_t_copied, 1)
            step = POOL_SLOTS[1] - POOL_SLOTS[0]
            for i in range(NBLK):
                act.wait_ge(s_query, i + 1)
                nc.scalar.copy(query_pool[:, i], ps_query[:, i, POOL_SLOTS[0]::step, :]).then_inc(s_query_pool, 1)

            def exponentials(i, h, first):
                g = GB * i + h
                act.wait_ge(s_shifted, g + 1)
                if not first:
                    act.wait_ge(s_sum_own, g + 1 - GB)
                for s in range(h * GT, h * GT + GT):
                    nc.scalar.activation(expd[:, s, :], scores[:, s, :], ACT.Exp,
                                         accum_out=exp_sum[:, s:s + 1]).then_inc(s_exp, 1)

            def take_out(i, n, first):
                act.wait_ge(s_weighted, BT * i + PT * (n + 1))
                if not (first and n < 2):
                    act.wait_ge(s_context_t, NPAIR * i + n - 1)
                for j in range(JW):
                    rows = slice(j * R, j * R + R)
                    nc.scalar.copy(context[rows, n % 2, :], ps_context[rows, n % 2, j * D:(j + 1) * D]) \
                        .then_inc(s_context, 1)

            def finish(i, first):
                act.wait_ge(s_context_t, NPAIR * (i + 1))
                nc.scalar.copy(context_t[:], ps_context_t).then_inc(s_context_t_copied, 1)
                act.wait_ge(s_project, i + 1)
                act.wait_ge(s_inv_sum, i + 1)
                if not first:
                    act.wait_ge(s_stored, 16 * i)
                nc.scalar.activation(result[:], ps_project, ACT.Copy, scale=inv_sum[:, 0:1]).then_inc(s_result, 1)
                act.wait_ge(s_result, i + 1)
                act.dma_start(out_blocks[i], result[:]).then_inc(s_stored, 16)

            def body(i, first, second):
                take_out(i - 1, 0, first)
                exponentials(i - 1, 1, first)
                take_out(i - 1, 1, first)
                take_out(i - 1, 2, first)
                exponentials(i, 0, False)
                take_out(i - 1, 3, first)
                finish(i - 1, first)

            exponentials(0, 0, True)
            body(1, True, True)
            with act.Fori(2, NBLK) as i:
                body(i, False, False)
            exponentials(NBLK - 1, 1, False)
            for n in range(NPAIR):
                take_out(NBLK - 1, n, False)
            finish(NBLK - 1, False)
            act.wait_ge(s_stored, 16 * NBLK)

        @block.vector
        def _(dve):
            nc.vector.memset(ones[:], 1.0).then_inc(s_ones, 1)
            dve.wait_ge(s_ident, 1)
            nc.vector.tensor_reduce(fold[:], ident[:].rearrange("p (j r) -> p r j", r=R), AX_X, ALU.add) \
                .then_inc(s_fold, 1)
            dve.wait_ge(s_small_t, 2)
            nc.vector.tensor_copy(w_target_t[:], ps_w_target_t).then_inc(s_small_t_copied, 1)
            nc.vector.tensor_copy(w_value_t[:], ps_w_value_t).then_inc(s_small_t_copied, 1)
            dve.wait_ge(s_mask, 16)
            nc.vector.tensor_scalar(mask_bias[:], mask_sb[:], -1.0, MASKED, ALU.add, ALU.mult).then_inc(s_mask_bias, 1)

            def score(i, s, first):
                t = BT * i + s
                if s in POOL_SLOTS:
                    dve.wait_ge(s_product_pool, pool_products(i, s))
                    prod = product_pool[:, POOL_SLOTS.index(s)]
                else:
                    dve.wait_ge(s_key[s], 16 * (i + 1))
                    if s == 0:
                        dve.wait_ge(s_query_pool, i + 1)
                    if not (first and s == 0):
                        dve.wait_ge(s_scores, t)
                    keys_s = key_ring[:, s, :].rearrange("p (j d) -> p j d", d=D)
                    query = ps_query[:, bass.ds(i, 1), s, :].to_broadcast([P, JL, D])
                    nc.vector.tensor_tensor(product[:], keys_s, query, ALU.mult).then_inc(s_product, 1)
                    dve.wait_ge(s_product, vector_products(i, s))
                    prod = product[:]
                if not first and s % GT == 0:
                    dve.wait_ge(s_exp, BT * (i - 1) + s + GT)
                nc.vector.tensor_reduce(scores[:, s, :], prod, AX_X, ALU.add).then_inc(s_scores, 1)

            def bias_and_chunk_max(i, h):
                g = GB * i + h
                rows = slice(h * GT, h * GT + GT)
                dve.wait_ge(s_scores, GT * (g + 1))
                if isinstance(i, int) and g == 0:
                    dve.wait_ge(s_mask_bias, 1)
                nc.vector.tensor_tensor(scores[:, rows, :], scores[:, rows, :],
                                        mask_bias[:, bass.ds(g * GT, GT), :], ALU.add).then_inc(s_biased, 1)
                dve.wait_ge(s_biased, g + 1)
                nc.vector.tensor_reduce(chunk_max[:, rows], scores[:, rows, :], AX_X, ALU.max).then_inc(s_chunk_max, 1)

            def user_maxima(g):
                dve.wait_ge(s_max_t, g + 1)
                nc.vector.tensor_reduce(user_max[:], ps_max_t.rearrange("t (b c) -> t b c", c=CH), AX_X,
                                        ALU.max).then_inc(s_user_max, 1)
                dve.wait_ge(s_user_max, g + 1)
                nc.vector.tensor_copy(user_max_rep[:], user_max[:].unsqueeze(2).to_broadcast([GT, TB, CH])) \
                    .then_inc(s_user_max_rep, 1)

            def shift(g, h):
                rows = slice(h * GT, h * GT + GT)
                dve.wait_ge(s_max_back, g + 1)
                nc.vector.tensor_tensor(scores[:, rows, :], scores[:, rows, :],
                                        ps_max_back.unsqueeze(2).to_broadcast([P, GT, JL]),
                                        ALU.subtract).then_inc(s_shifted, 1)

            def invert_sums(i, first):
                dve.wait_ge(s_sum, i + 1)
                if not first:
                    dve.wait_ge(s_result, i)
                nc.vector.reciprocal(inv_sum[:], ps_sum).then_inc(s_inv_sum, 1)

            def step(i, s, first, second):
                score(i, s, first)
                if s == 0 and not first:
                    user_maxima(GB * i - 1)
                if s == 1 and not first:
                    shift(GB * i - 1, GB - 1)
                if s == GT:
                    user_maxima(GB * i)
                if s == 1 + GT:
                    shift(GB * i, 0)
                if s == BT - 1 and not first:
                    invert_sums(i - 1, second)
                if s % GT == GT - 1:
                    bias_and_chunk_max(i, s // GT)

            for s in range(BT):
                step(0, s, True, False)
            for s in range(BT):
                step(1, s, False, True)
            with dve.Fori(2, NBLK) as i:
                for s in range(BT):
                    step(i, s, False, False)
            user_maxima(GB * NBLK - 1)
            shift(GB * NBLK - 1, GB - 1)
            invert_sums(NBLK - 1, False)

        @block.tensor
        def _(pe):
            pe.wait_ge(s_ident, 1)
            pe.wait_ge(s_targets, 16)
            for n in range(B // P):
                last = nc.tensor.transpose(ps_target_t[:, n * P:(n + 1) * P], target_sb[:, n, :], ident[:])
            last.then_inc(s_small_t, 1)
            pe.wait_ge(s_weights, 16 * 3)
            nc.tensor.transpose(ps_w_target_t, w_target_sb[:], ident[0:D, 0:D])
            nc.tensor.transpose(ps_w_value_t, w_value_sb[:], ident[0:D, 0:D]).then_inc(s_small_t, 1)
            pe.wait_ge(s_small_t_copied, 3)
            nc.tensor.matmul(ps_query_t, w_target_t[:], target_t[:], start=True, stop=True).then_inc(s_query_t, 1)
            for i in range(NBLK):
                pe.wait_ge(s_query_t_copied, i + 1)
                for s in range(BT):
                    users = query_t[:, i, s * TB:(s + 1) * TB, :].rearrange("e b c -> e (b c)")
                    last = nc.tensor.matmul(ps_query[:, i, s, :], users, w_item_sb[:], start=True, stop=True)
                last.then_inc(s_query, 1)

            def weigh_values(i, s, first):
                pe.wait_ge(s_value[s], 16 * (i + 1))
                pe.wait_ge(s_spread, BT * i + s + 1)
                if s % PT == 0 and not (first and s < 2 * PT):
                    pe.wait_ge(s_context, JW * (NPAIR * i + s // PT - 1))
                for k in [*range(NW - 2), NW - 1, NW - 2]:
                    cols = slice(k * JW * D, min((k + 1) * JW, JL) * D)
                    last = nc.tensor.matmul(
                        ps_context[:, s // PT % 2, 0:cols.stop - cols.start],
                        weights[:, s, k * JW:(k + 1) * JW, :].rearrange("p j r -> p (j r)"),
                        value_ring[:, s, cols], start=(k == 0 and s % PT == 0),
                        stop=(k == NW - 2 and s % PT == PT - 1))
                last.then_inc(s_weighted, 1)

            def fold_context(i, n, first):
                pe.wait_ge(s_context, JW * (NPAIR * i + n + 1))
                if n == 0 and not first:
                    pe.wait_ge(s_result, i)
                nc.tensor.matmul(ps_context_t[:, n * R:(n + 1) * R], context[:, n % 2, :], fold[:],
                                 start=True, stop=True).then_inc(s_context_t, 1)

            def project(i):
                pe.wait_ge(s_context_t_copied, i + 1)
                nc.tensor.matmul(ps_project, context_t[:], w_value_t[:], start=True, stop=True).then_inc(s_project, 1)

            def turn_maxima(g, h):
                pe.wait_ge(s_chunk_max, g + 1)
                nc.tensor.matmul(ps_max_t, chunk_max[:, h * GT:(h + 1) * GT], ident[:],
                                 start=True, stop=True).then_inc(s_max_t, 1)

            def turn_back(g):
                pe.wait_ge(s_user_max_rep, g + 1)
                nc.tensor.matmul(ps_max_back, user_max_rep[:].rearrange("t b c -> t (b c)"), ident[0:GT, 0:GT],
                                 start=True, stop=True).then_inc(s_max_back, 1)

            def sum_by_user(i, shifted):
                pe.wait_ge(s_sum_own, GB * (i + 1))
                pe.wait_ge(s_shifted, shifted)
                nc.tensor.matmul(ps_sum, exp_sum_own[:].rearrange("p s b -> p (s b)"), ones[:],
                                 start=True, stop=True).then_inc(s_sum, 1)

            def body(i, first):
                for s in range(BT):
                    if s == 0:
                        turn_maxima(GB * i - 1, GB - 1)
                    if s == 1:
                        turn_back(GB * i - 1)
                    if s == GT:
                        turn_maxima(GB * i, 0)
                    if s == 1 + GT:
                        turn_back(GB * i)
                    if s == 2 + GT:
                        sum_by_user(i - 1, GB * i + 1)
                    weigh_values(i - 1, s, first)
                    if s % PT == 0 and s > 0:
                        fold_context(i - 1, s // PT - 1, first)
                fold_context(i - 1, NPAIR - 1, first)
                project(i - 1)

            pe.wait_ge(s_fold, 1)
            pe.wait_ge(s_ones, 1)
            turn_maxima(0, 0)
            turn_back(0)
            body(1, True)
            with pe.Fori(2, NBLK) as i:
                body(i, False)
            for s in range(BT):
                weigh_values(NBLK - 1, s, False)
                if s == 0:
                    turn_maxima(GB * NBLK - 1, GB - 1)
                if s == 1:
                    turn_back(GB * NBLK - 1)
                if s == BT - 2:
                    sum_by_user(NBLK - 1, GB * NBLK)
                if s % PT == 0 and s > 0:
                    fold_context(NBLK - 1, s // PT - 1, False)
            fold_context(NBLK - 1, NPAIR - 1, False)
            project(NBLK - 1)


_INS = ["r_target_key", "r_item_keys", "r_item_values", "r_mask", "L0_rec_W_target", "L0_rec_W_item", "L0_rec_W_value"]


def kernel(**inputs):
    import numpy as np
    import concourse.bacc as bacc
    from concourse.bass_utils import run_bass_kernel_spmd

    nc = bacc.Bacc("TRN2", target_bir_lowering=False, num_devices=1)
    arrays, args = {}, []
    for name in _INS:
        a = np.ascontiguousarray(inputs[name])
        arrays[f"{name}_dram"] = a
        args.append(nc.dram_tensor(f"{name}_dram", a.shape, mybir.dt.from_np(a.dtype), kind="ExternalInput").ap())
    shape = inputs["r_target_key"].shape
    out = nc.dram_tensor("out_dram", shape, F32, kind="ExternalOutput").ap()
    masked_attention_kernel(nc, *args, out)
    r = run_bass_kernel_spmd(nc, [arrays], core_ids=[0])
    return r.results[0]["out_dram"]
```

```python
from contextlib import ExitStack

import concourse.bass as bass
from concourse import mybir

ALU = mybir.AluOpType
ACT = mybir.ActivationFunctionType
F32 = mybir.dt.float32
AX_X = mybir.AxisListType.X

P = 128
CH = 8
TB = P // CH
BT = 8
GT = 4
GB = BT // GT
JW = 4
PT = 2
POOL_SLOTS = (2, 6)
VECTOR_SLOTS = (2, 4)
SPLIT_SLOTS = {6: 12, 7: 12}
FIRST_TILES = 2
MASKED = 1.0e8


def masked_attention_kernel(nc, target_cols, keys, values, mask_rows, w_target, w_item, w_value_cols, out):
    B, L, D = keys.shape
    JL = L // CH
    NW = -(-JL // JW)
    NT = B // TB
    NBLK = NT // BT
    UB = BT * TB
    R = PT * TB
    NPAIR = BT // PT
    NPOOL = len(POOL_SLOTS)
    NVEC = BT - NPOOL
    assert JL * CH == L and NT % BT == 0 and UB == P and R * JW == P and NBLK >= 3
    NPARTIAL = len(VECTOR_SLOTS) + len(SPLIT_SLOTS)
    assert tuple(SPLIT_SLOTS) == (BT - 2, BT - 1) and all(cut % JW == 0 for cut in SPLIT_SLOTS.values())
    assert JL - (NW - 1) * JW == 1 and BT * D == 512

    keys_tiled = keys.rearrange("(t b) (c j) d -> t (b c) (j d)", b=TB, c=CH)
    values_tiled = values.rearrange("(t b) (c j) d -> t (b c) (j d)", b=TB, c=CH)
    out_blocks = out.rearrange("(n u) d -> n u d", u=UB)

    def vector_products(i, s):
        return NVEC * i + len([x for x in range(s + 1) if x not in POOL_SLOTS])

    def pool_products(i, s):
        return NPOOL * i + len([x for x in range(s + 1) if x in POOL_SLOTS])

    with ExitStack() as ctx:
        def sb(name, shape, dt=F32):
            return ctx.enter_context(nc.sbuf_tensor(name, shape, dt))

        def psum(name, shape):
            return ctx.enter_context(nc.psum_tensor(name, shape, F32))

        def sem(name):
            return ctx.enter_context(nc.semaphore(name))

        key_ring = sb("key_ring", [P, BT, JL * D])
        value_ring = sb("value_ring", [P, BT, JL * D])
        ident = sb("ident", [P, P])
        own_user = sb("own_user", [P, TB])
        fold = sb("fold", [P, R])
        ones = sb("ones", [P, 1])
        w_target_sb = sb("w_target_sb", [D, D])
        w_item_sb = sb("w_item_sb", [D, D])
        w_value_t = sb("w_value_t", [D, D])
        w_both = sb("w_both", [D, D])
        target_t = sb("target_t", [D, NBLK, UB])
        target_rep = sb("target_rep", [D, NBLK, UB, CH])
        query_first = sb("query_first", [P, BT, D])
        query_pool = sb("query_pool", [P, NBLK, NPOOL, D])
        mask_sb = sb("mask_sb", [P, NT, JL], mask_rows.dtype)
        mask_bias = sb("mask_bias", [P, NT, JL])
        product = sb("product", [P, JL, D])
        product_pool = sb("product_pool", [P, NPOOL, JL, D])
        scores = sb("scores", [P, BT, JL])
        chunk_max = sb("chunk_max", [P, BT])
        user_max = sb("user_max", [GT, TB])
        user_max_rep = sb("user_max_rep", [GT, TB, CH])
        expd = sb("expd", [P, BT, JL])
        exp_sum = sb("exp_sum", [P, BT])
        weights = sb("weights", [P, BT, NW * JW, R])
        partial = sb("partial", [P, NPARTIAL, D])
        exp_sum_own = sb("exp_sum_own", [P, BT, TB])
        context = sb("context", [P, 2, D])
        context_t = sb("context_t", [D, UB])
        inv_sum = sb("inv_sum", [P, 1])
        result = sb("result", [P, NBLK, D])

        ps_query = psum("ps_query", [P, NBLK - 1, BT, D])
        ps_context = psum("ps_context", [P, 2, 512])
        ps_small = psum("ps_small", [P, 512])
        ps_out = psum("ps_out", [P, 512])
        ps_max_t = ps_small[0:GT, 0:P]
        ps_max_back = ps_small[:, P:P + GT]
        ps_sum = ps_small[:, P + GT:P + GT + 1]
        ps_w_both = ps_small[0:D, 256:256 + D]
        ps_context_t = ps_out[0:D, 0:UB]
        ps_project = ps_out[:, UB:UB + D]

        s_targets = sem("s_targets")
        s_weights = sem("s_weights")
        s_w_value = sem("s_w_value")
        s_mask = sem("s_mask")
        s_key = [sem(f"s_key{s}") for s in range(BT)]
        s_value = [sem(f"s_value{s}") for s in range(BT)]
        s_value_rest = sem("s_value_rest")
        s_fill = sem("s_fill")
        s_ident = sem("s_ident")
        s_own = sem("s_own")
        s_ones = sem("s_ones")
        s_fold = sem("s_fold")
        s_both = sem("s_both")
        s_both_copied = sem("s_both_copied")
        s_rep = sem("s_rep")
        s_rep_first = sem("s_rep_first")
        s_query_first = sem("s_query_first")
        s_query_first_copied = sem("s_query_first_copied")
        s_query = sem("s_query")
        s_query_pool = sem("s_query_pool")
        s_mask_bias = sem("s_mask_bias")
        s_product = sem("s_product")
        s_product_pool = sem("s_product_pool")
        s_scores = sem("s_scores")
        s_biased = sem("s_biased")
        s_chunk_max = sem("s_chunk_max")
        s_max_t = sem("s_max_t")
        s_user_max = sem("s_user_max")
        s_user_max_rep = sem("s_user_max_rep")
        s_max_back = sem("s_max_back")
        s_shifted = sem("s_shifted")
        s_exp = sem("s_exp")
        s_spread = sem("s_spread")
        s_sum_own = sem("s_sum_own")
        s_value_product = sem("s_value_product")
        s_partial = sem("s_partial")
        s_weighted = sem("s_weighted")
        s_context = sem("s_context")
        s_context_t = sem("s_context_t")
        s_folded = sem("s_folded")
        s_context_t_copied = sem("s_context_t_copied")
        s_sum = sem("s_sum")
        s_inv_sum = sem("s_inv_sum")
        s_project = sem("s_project")
        s_result = sem("s_result")
        s_stored = sem("s_stored")

        block = ctx.enter_context(nc.Block())

        @block.sync
        def _(sp):
            def load_key(i, s, first):
                if not first and s in POOL_SLOTS:
                    sp.wait_ge(s_product_pool, pool_products(i - 1, s))
                elif not first:
                    sp.wait_ge(s_product, vector_products(i - 1, s))
                sp.dma_start(key_ring[:, s, :], keys_tiled[i * BT + s]).then_inc(s_key[s], 16)

            def load_value(i, s, first):
                if not first:
                    sp.wait_ge(s_weighted, BT * (i - 1) + s + 1)
                sp.dma_start(value_ring[:, s, :], values_tiled[i * BT + s]).then_inc(s_value[s], 16)

            load_key(0, 0, True)
            sp.dma_start(w_target_sb[:], w_target).then_inc(s_weights, 16)
            sp.dma_start(w_item_sb[:], w_item).then_inc(s_weights, 16)
            sp.dma_start(target_t[:], target_cols.rearrange("d (n u) -> d n u", u=UB)).then_inc(s_targets, 16)
            for s in range(1, BT):
                load_key(0, s, True)
            for s in range(BT):
                load_key(1, s, False)
                load_value(0, s, True)
            with sp.Fori(2, NBLK) as i:
                for s in range(BT):
                    load_key(i, s, False)
                    load_value(i - 1, s, False)
            for s in range(BT - 1):
                load_value(NBLK - 1, s, False)
            sp.wait_ge(s_weighted, BT * (NBLK - 1))
            cut = SPLIT_SLOTS[BT - 1] * D
            sp.dma_start(value_ring[:, BT - 1, 0:cut], values_tiled[NT - 1][:, 0:cut]).then_inc(s_value[BT - 1], 16)
            sp.dma_start(value_ring[:, BT - 1, cut:], values_tiled[NT - 1][:, cut:]).then_inc(s_value_rest, 16)

        @block.gpsimd
        def _(pool):
            nc.gpsimd.memset(ident[:], 0.0).then_inc(s_fill, 1)
            pool.wait_ge(s_fill, 1)
            nc.gpsimd.affine_select(out=ident[:], in_=ident[:], compare_op=ALU.not_equal, fill=1.0, base=0,
                                    pattern=[[-1, P]], channel_multiplier=1).then_inc(s_ident, 1)
            nc.gpsimd.memset(own_user[:], 1.0).then_inc(s_fill, 1)
            pool.wait_ge(s_fill, 2)
            nc.gpsimd.affine_select(out=own_user[:], in_=own_user[:], compare_op=ALU.is_ge, fill=0.0, base=0,
                                    pattern=[[-CH, TB]], channel_multiplier=1).then_inc(s_fill, 1)
            pool.wait_ge(s_fill, 3)
            nc.gpsimd.affine_select(out=own_user[:], in_=own_user[:], compare_op=ALU.is_ge, fill=0.0, base=CH - 1,
                                    pattern=[[CH, TB]], channel_multiplier=-1).then_inc(s_own, 1)
            nc.gpsimd.memset(weights[:], 0.0).then_inc(s_fill, 1)
            pool.wait_ge(s_own, 1)
            pool.wait_ge(s_fill, 4)

            def multiply(i, n, first):
                s = POOL_SLOTS[n]
                pool.wait_ge(s_key[s], 16 * (i + 1))
                if first:
                    pool.wait_ge(s_query_first_copied, 2)
                    query = query_first[:, s:s + 1, :].to_broadcast([P, JL, D])
                else:
                    pool.wait_ge(s_scores, BT * (i - 1) + s + 1)
                    pool.wait_ge(s_query_pool, NBLK - 1)
                    query = query_pool[:, bass.ds(i, 1), n, :].to_broadcast([P, JL, D])
                keys_s = key_ring[:, s, :].rearrange("p (j d) -> p j d", d=D)
                nc.gpsimd.tensor_tensor(product_pool[:, n], keys_s, query, ALU.mult).then_inc(s_product_pool, 1)

            def spread(i, h, first):
                g = GB * i + h
                pool.wait_ge(s_exp, GT * (g + 1))
                for s in range(h * GT, h * GT + GT):
                    if not first:
                        pool.wait_ge(s_weighted, BT * (i - 1) + s + 1)
                    users = slice(s % PT * TB, s % PT * TB + TB)
                    nc.gpsimd.tensor_tensor(
                        weights[:, s, 0:JL, users], expd[:, s, :].unsqueeze(2).to_broadcast([P, JL, TB]),
                        own_user[:].unsqueeze(1).to_broadcast([P, JL, TB]), ALU.mult).then_inc(s_spread, 1)
                rows = slice(h * GT, h * GT + GT)
                if not first:
                    pool.wait_ge(s_sum, i)
                nc.gpsimd.tensor_tensor(
                    exp_sum_own[:, rows, :], exp_sum[:, rows].unsqueeze(2).to_broadcast([P, GT, TB]),
                    own_user[:].unsqueeze(1).to_broadcast([P, GT, TB]), ALU.mult).then_inc(s_sum_own, 1)

            multiply(0, 0, True)
            multiply(0, 1, True)
            spread(0, 0, True)
            multiply(1, 0, False)
            spread(0, 1, True)
            multiply(1, 1, False)
            spread(1, 0, False)
            with pool.Fori(2, NBLK) as i:
                multiply(i, 0, False)
                spread(i - 1, 1, False)
                multiply(i, 1, False)
                spread(i, 0, False)
            spread(NBLK - 1, 1, False)

        @block.scalar
        def _(act):
            act.dma_start(w_value_t[:], w_value_cols).then_inc(s_w_value, 16)
            act.dma_start(mask_sb[:], mask_rows).then_inc(s_mask, 16)

            act.wait_ge(s_both, 1)
            nc.scalar.mul(w_both[:], ps_w_both, float(D) ** -0.5).then_inc(s_both_copied, 1)
            act.wait_ge(s_targets, 16)
            for i in range(1, NBLK):
                nc.scalar.copy(target_rep[:, i], target_t[:, i].unsqueeze(2).to_broadcast([D, UB, CH])) \
                    .then_inc(s_rep, 1)
            for n, tiles in enumerate((slice(0, FIRST_TILES), slice(FIRST_TILES, BT))):
                act.wait_ge(s_query_first, n + 1)
                nc.scalar.copy(query_first[:, tiles, :],
                               ps_context[:, n, 0:(tiles.stop - tiles.start) * D].rearrange("p (s d) -> p s d", d=D)) \
                    .then_inc(s_query_first_copied, 1)
            step = POOL_SLOTS[1] - POOL_SLOTS[0]
            for i in range(1, NBLK):
                act.wait_ge(s_query, i)
                nc.scalar.copy(query_pool[:, i], ps_query[:, i - 1, POOL_SLOTS[0]::step, :]).then_inc(s_query_pool, 1)

            def exponentials(i, h, first):
                g = GB * i + h
                act.wait_ge(s_shifted, g + 1)
                if not first:
                    act.wait_ge(s_sum_own, g + 1 - GB)
                for s in range(h * GT, h * GT + GT):
                    nc.scalar.activation(expd[:, s, :], scores[:, s, :], ACT.Exp,
                                         accum_out=exp_sum[:, s:s + 1]).then_inc(s_exp, 1)

            def take_out(i, n, first, last_block=False):
                skipped = len([x for x in VECTOR_SLOTS if last_block and x < PT * (n + 1)])
                act.wait_ge(s_weighted, BT * i + PT * (n + 1) - skipped)
                if not (first and n < 2):
                    act.wait_ge(s_context_t, NPAIR * i + n - 1)
                for j in range(JW):
                    rows = slice(j * R, j * R + R)
                    nc.scalar.copy(context[rows, n % 2, :], ps_context[rows, n % 2, j * D:(j + 1) * D]) \
                        .then_inc(s_context, 1)

            def finish(i):
                act.wait_ge(s_context_t, NPAIR * (i + 1))
                nc.scalar.copy(context_t[:], ps_context_t).then_inc(s_context_t_copied, 1)
                act.wait_ge(s_project, i + 1)
                act.wait_ge(s_inv_sum, i + 1)
                rows = result[:, bass.ds(i, 1), :].rearrange("p n d -> p (n d)")
                nc.scalar.activation(rows, ps_project, ACT.Copy, scale=inv_sum[:, 0:1]).then_inc(s_result, 1)
                act.wait_ge(s_result, i + 1)
                act.dma_start(out_blocks[i], rows).then_inc(s_stored, 16)

            def body(i, first):
                take_out(i - 1, 0, first)
                exponentials(i - 1, 1, first)
                take_out(i - 1, 1, first)
                take_out(i - 1, 2, first)
                exponentials(i, 0, False)
                take_out(i - 1, 3, first)

            exponentials(0, 0, True)
            body(1, True)
            with act.Fori(2, NBLK) as i:
                finish(i - 2)
                body(i, False)
            exponentials(NBLK - 1, 1, False)
            finish(NBLK - 2)
            for n in range(NPAIR):
                take_out(NBLK - 1, n, False, True)
            act.wait_ge(s_folded, NPARTIAL)
            finish(NBLK - 1)
            act.wait_ge(s_stored, 16 * NBLK)

        @block.vector
        def _(dve):
            nc.vector.memset(ones[:], 1.0).then_inc(s_ones, 1)
            dve.wait_ge(s_ident, 1)
            nc.vector.tensor_reduce(fold[:], ident[:].rearrange("p (j r) -> p r j", r=R), AX_X, ALU.add) \
                .then_inc(s_fold, 1)
            dve.wait_ge(s_targets, 16)
            nc.vector.tensor_copy(target_rep[:, 0], target_t[:, 0].unsqueeze(2).to_broadcast([D, UB, CH])) \
                .then_inc(s_rep_first, 1)
            dve.wait_ge(s_mask, 16)
            nc.vector.tensor_scalar(mask_bias[:], mask_sb[:], -1.0, MASKED, ALU.add, ALU.mult).then_inc(s_mask_bias, 1)

            def score(i, s, first):
                t = BT * i + s
                if s in POOL_SLOTS:
                    dve.wait_ge(s_product_pool, pool_products(i, s))
                    prod = product_pool[:, POOL_SLOTS.index(s)]
                else:
                    dve.wait_ge(s_key[s], 16 * (i + 1))
                    if first:
                        dve.wait_ge(s_query_first_copied, 1 if s < FIRST_TILES else 2)
                        query = query_first[:, s:s + 1, :].to_broadcast([P, JL, D])
                    else:
                        if s == 0:
                            dve.wait_ge(s_query_pool, NBLK - 1)
                        query = ps_query[:, bass.ds(i - 1, 1), s, :].to_broadcast([P, JL, D])
                    if not (first and s == 0):
                        dve.wait_ge(s_scores, t)
                    keys_s = key_ring[:, s, :].rearrange("p (j d) -> p j d", d=D)
                    nc.vector.tensor_tensor(product[:], keys_s, query, ALU.mult).then_inc(s_product, 1)
                    dve.wait_ge(s_product, vector_products(i, s))
                    prod = product[:]
                if not first and s % GT == 0:
                    dve.wait_ge(s_exp, BT * (i - 1) + s + GT)
                nc.vector.tensor_reduce(scores[:, s, :], prod, AX_X, ALU.add).then_inc(s_scores, 1)

            def bias_and_chunk_max(i, h):
                g = GB * i + h
                rows = slice(h * GT, h * GT + GT)
                dve.wait_ge(s_scores, GT * (g + 1))
                if isinstance(i, int) and g == 0:
                    dve.wait_ge(s_mask_bias, 1)
                nc.vector.tensor_tensor(scores[:, rows, :], scores[:, rows, :],
                                        mask_bias[:, bass.ds(g * GT, GT), :], ALU.add).then_inc(s_biased, 1)
                dve.wait_ge(s_biased, g + 1)
                nc.vector.tensor_reduce(chunk_max[:, rows], scores[:, rows, :], AX_X, ALU.max).then_inc(s_chunk_max, 1)

            def user_maxima(g):
                dve.wait_ge(s_max_t, g + 1)
                nc.vector.tensor_reduce(user_max[:], ps_max_t.rearrange("t (b c) -> t b c", c=CH), AX_X,
                                        ALU.max).then_inc(s_user_max, 1)
                dve.wait_ge(s_user_max, g + 1)
                nc.vector.tensor_copy(user_max_rep[:], user_max[:].unsqueeze(2).to_broadcast([GT, TB, CH])) \
                    .then_inc(s_user_max_rep, 1)

            def shift(g, h):
                rows = slice(h * GT, h * GT + GT)
                dve.wait_ge(s_max_back, g + 1)
                nc.vector.tensor_tensor(scores[:, rows, :], scores[:, rows, :],
                                        ps_max_back.unsqueeze(2).to_broadcast([P, GT, JL]),
                                        ALU.subtract).then_inc(s_shifted, 1)

            def invert_sums(i, first):
                dve.wait_ge(s_sum, i + 1)
                if not first:
                    dve.wait_ge(s_result, i)
                nc.vector.reciprocal(inv_sum[:], ps_sum).then_inc(s_inv_sum, 1)

            def step(i, s, first, second):
                score(i, s, first)
                if s == 0 and not first:
                    user_maxima(GB * i - 1)
                if s == 1 and not first:
                    shift(GB * i - 1, GB - 1)
                if s == GT:
                    user_maxima(GB * i)
                if s == 1 + GT:
                    shift(GB * i, 0)
                if s == BT - 1 and not first:
                    invert_sums(i - 1, second)
                if s % GT == GT - 1:
                    bias_and_chunk_max(i, s // GT)

            for s in range(BT):
                step(0, s, True, False)
            for s in range(BT):
                step(1, s, False, True)
            with dve.Fori(2, NBLK) as i:
                for s in range(BT):
                    step(i, s, False, False)
            user_maxima(GB * NBLK - 1)
            shift(GB * NBLK - 1, GB - 1)

            def sum_values(n, s, items):
                dve.wait_ge(s_exp, BT * (NBLK - 1) + s + 1)
                if n == 0:
                    dve.wait_ge(s_scores, NT)
                else:
                    dve.wait_ge(s_partial, n)
                count = items.stop - items.start
                nc.vector.tensor_tensor(
                    product[:, items, :], value_ring[:, s, :].rearrange("p (j d) -> p j d", d=D)[:, items, :],
                    expd[:, s, items].unsqueeze(2).to_broadcast([P, count, D]), ALU.mult).then_inc(s_value_product, 1)
                dve.wait_ge(s_value_product, n + 1)
                nc.vector.tensor_reduce(partial[:, n, :], product[:, items, :].rearrange("p j d -> p d j"), AX_X,
                                        ALU.add).then_inc(s_partial, 1)

            for n, s in enumerate(VECTOR_SLOTS):
                dve.wait_ge(s_value[s], 16 * NBLK)
                sum_values(n, s, slice(0, JL))
            dve.wait_ge(s_value[BT - 2], 16 * NBLK)
            sum_values(NPARTIAL - 2, BT - 2, slice(SPLIT_SLOTS[BT - 2], JL))
            invert_sums(NBLK - 1, False)
            dve.wait_ge(s_value_rest, 16)
            sum_values(NPARTIAL - 1, BT - 1, slice(SPLIT_SLOTS[BT - 1], JL))

        @block.tensor
        def _(pe):
            pe.wait_ge(s_weights, 32)
            nc.tensor.matmul(ps_w_both, w_target_sb[:], w_item_sb[:], start=True, stop=True).then_inc(s_both, 1)

            def query(dst, i, s):
                return nc.tensor.matmul(dst, target_rep[:, i, s * TB:(s + 1) * TB, :].rearrange("d b c -> d (b c)"),
                                        w_both[:], start=True, stop=True)

            pe.wait_ge(s_both_copied, 1)
            pe.wait_ge(s_rep_first, 1)
            for n, tiles in enumerate((range(FIRST_TILES), range(FIRST_TILES, BT))):
                for s in tiles:
                    c = (s - tiles.start) * D
                    last = query(ps_context[:, n, c:c + D], 0, s)
                last.then_inc(s_query_first, 1)
            for i in range(1, NBLK):
                pe.wait_ge(s_rep, i)
                for s in range(BT):
                    last = query(ps_query[:, i - 1, s, :], i, s)
                last.then_inc(s_query, 1)

            every_four = [*range(NW - 2), NW - 1, NW - 2]

            def weigh_values(i, s, first, start=None, stop=None, fours=every_four):
                start = s % PT == 0 if start is None else start
                stop = s % PT == PT - 1 if stop is None else stop
                pe.wait_ge(s_value[s], 16 * (i + 1))
                pe.wait_ge(s_spread, BT * i + s + 1)
                if start and not (first and s < 2 * PT):
                    pe.wait_ge(s_context, JW * (NPAIR * i + s // PT - 1))
                for k in fours:
                    cols = slice(k * JW * D, min((k + 1) * JW, JL) * D)
                    last = nc.tensor.matmul(
                        ps_context[:, s // PT % 2, 0:cols.stop - cols.start],
                        weights[:, s, k * JW:(k + 1) * JW, :].rearrange("p j r -> p (j r)"),
                        value_ring[:, s, cols], start=(k == fours[0] and start), stop=(k == fours[-1] and stop))
                last.then_inc(s_weighted, 1)

            def fold_context(i, n, first):
                pe.wait_ge(s_context, JW * (NPAIR * i + n + 1))
                if n == 0 and not first:
                    pe.wait_ge(s_result, i)
                nc.tensor.matmul(ps_context_t[:, n * R:(n + 1) * R], context[:, n % 2, :], fold[:],
                                 start=True, stop=True).then_inc(s_context_t, 1)

            def fold_last_context(n):
                pe.wait_ge(s_context, JW * (NPAIR * (NBLK - 1) + n + 1))
                if n == 0:
                    pe.wait_ge(s_result, NBLK - 1)
                tiles = [s for s in range(n * PT, (n + 1) * PT) if s not in VECTOR_SLOTS]
                first, past = tiles[0], tiles[-1] + 1
                nc.tensor.matmul(ps_context_t[:, first * TB:past * TB], context[:, n % 2, :],
                                 fold[:, (first - n * PT) * TB:(past - n * PT) * TB], start=True,
                                 stop=n < NPAIR - 1).then_inc(s_context_t, 1)

            def fold_partial(n, s):
                pe.wait_ge(s_partial, n + 1)
                nc.tensor.matmul(ps_context_t[:, s * TB:(s + 1) * TB], partial[:, n, :], own_user[:],
                                 start=s not in SPLIT_SLOTS, stop=s != BT - 2).then_inc(s_folded, 1)

            def project(i):
                pe.wait_ge(s_context_t_copied, i + 1)
                nc.tensor.matmul(ps_project, context_t[:], w_value_t[:], start=True, stop=True).then_inc(s_project, 1)

            def turn_maxima(g, h):
                pe.wait_ge(s_chunk_max, g + 1)
                nc.tensor.matmul(ps_max_t, chunk_max[:, h * GT:(h + 1) * GT], ident[:],
                                 start=True, stop=True).then_inc(s_max_t, 1)

            def turn_back(g):
                pe.wait_ge(s_user_max_rep, g + 1)
                nc.tensor.matmul(ps_max_back, user_max_rep[:].rearrange("t b c -> t (b c)"), ident[0:GT, 0:GT],
                                 start=True, stop=True).then_inc(s_max_back, 1)

            def sum_by_user(i, shifted):
                pe.wait_ge(s_sum_own, GB * (i + 1))
                pe.wait_ge(s_shifted, shifted)
                nc.tensor.matmul(ps_sum, exp_sum_own[:].rearrange("p s b -> p (s b)"), ones[:],
                                 start=True, stop=True).then_inc(s_sum, 1)

            def body(i, first):
                for s in range(BT):
                    if s == 0:
                        turn_maxima(GB * i - 1, GB - 1)
                    if s == 1:
                        turn_back(GB * i - 1)
                    if s == GT:
                        turn_maxima(GB * i, 0)
                    if s == 1 + GT:
                        turn_back(GB * i)
                    if s == 2 + GT:
                        sum_by_user(i - 1, GB * i + 1)
                    weigh_values(i - 1, s, first)
                    if s % PT == 0 and s > 0:
                        fold_context(i - 1, s // PT - 1, first)
                    if s == 0 and not first:
                        fold_context(i - 2, NPAIR - 1, False)
                    if s == 1 and not first:
                        project(i - 2)

            pe.wait_ge(s_ident, 1)
            pe.wait_ge(s_own, 1)
            pe.wait_ge(s_fold, 1)
            pe.wait_ge(s_ones, 1)
            pe.wait_ge(s_w_value, 16)
            turn_maxima(0, 0)
            turn_back(0)
            body(1, True)
            with pe.Fori(2, NBLK) as i:
                body(i, False)
            turn_maxima(GB * NBLK - 1, GB - 1)
            weigh_values(NBLK - 1, 0, False)
            fold_context(NBLK - 2, NPAIR - 1, False)
            turn_back(GB * NBLK - 1)
            weigh_values(NBLK - 1, 1, False)
            project(NBLK - 2)
            for s in range(2, BT - 2):
                if s not in VECTOR_SLOTS:
                    alone = s // PT in [x // PT for x in VECTOR_SLOTS]
                    weigh_values(NBLK - 1, s, False, True if alone else None, True if alone else None)
                if s % PT == 1:
                    fold_last_context(s // PT - 1)
            sum_by_user(NBLK - 1, GB * NBLK)
            for s, cut in SPLIT_SLOTS.items():
                weigh_values(NBLK - 1, s, False, fours=range(cut // JW))
            fold_last_context(NPAIR - 2)
            for n, s in enumerate(VECTOR_SLOTS):
                fold_partial(n, s)
            fold_last_context(NPAIR - 1)
            for n, s in enumerate(SPLIT_SLOTS):
                fold_partial(len(VECTOR_SLOTS) + n, s)
            project(NBLK - 1)


def kernel(**inputs):
    import numpy as np
    import concourse.bacc as bacc
    from concourse.bass_utils import run_bass_kernel_spmd

    target, mask = np.asarray(inputs["r_target_key"]), np.asarray(inputs["r_mask"])
    arrays = {
        "target_cols": target.T,
        "keys": inputs["r_item_keys"],
        "values": inputs["r_item_values"],
        "mask_rows": mask.reshape(mask.shape[0] // TB, P, mask.shape[1] // CH).transpose(1, 0, 2),
        "w_target": inputs["L0_rec_W_target"],
        "w_item": inputs["L0_rec_W_item"],
        "w_value_cols": np.asarray(inputs["L0_rec_W_value"]).T,
    }
    arrays = {name: np.ascontiguousarray(a) for name, a in arrays.items()}
    nc = bacc.Bacc("TRN2", target_bir_lowering=False, num_devices=1)
    args = [nc.dram_tensor(name, a.shape, mybir.dt.from_np(a.dtype), kind="ExternalInput").ap()
            for name, a in arrays.items()]
    out = nc.dram_tensor("out", target.shape, F32, kind="ExternalOutput").ap()
    masked_attention_kernel(nc, *args, out)
    r = run_bass_kernel_spmd(nc, [arrays], core_ids=[0])
    return r.results[0]["out"]
```
